# Optimizing a Trainium2 kernel written in Bass

```python
import numpy as np
import jax
import jax.numpy as jnp

def _softmax(x, axis=-1):
    return jax.nn.softmax(x, axis=axis)

def _gelu(x):
    return jax.nn.gelu(x, approximate=True)

def _silu(x):
    return jax.nn.silu(x)

def _sigmoid(x):
    return jax.nn.sigmoid(x)

def _layernorm(x, axis=-1, eps=1e-05):
    m = jnp.mean(x, axis=axis, keepdims=True)
    v = jnp.var(x, axis=axis, keepdims=True)
    return (x - m) / jnp.sqrt(v + eps)

def _scatter_add(tgt, idx, src, axis=0):
    return tgt.at[idx].add(src)

def _segment_sum(src, seg, n):
    return jax.ops.segment_sum(src, seg, n)
kernel_name = 'mk_dlrm_tower_d1_rec_r8_13f8ab'

def setup_inputs(seed: int=0):
    np.random.seed(seed)
    _w = jnp.asarray

    def _rec_inputs():
        import jax
        import jax.numpy as jnp
        _tk = jax.random.key(seed)
        dense_ctx = jax.random.normal(jax.random.fold_in(_tk, 190), (2048, 16), jnp.float32)
        ids = jnp.stack([jax.random.randint(jax.random.fold_in(_tk, 200 + f), (2048,), 0, v, jnp.int32) for f, v in enumerate([125000, 1000, 1250, 1250, 12500, 1000, 12500, 1000, 1000, 1250, 1250, 12500, 12500, 1000, 12500, 12500, 1000, 1250, 1000, 1000, 1000, 1250, 1000, 12500, 1250, 1000, 12500])], axis=1)
        tbl_0 = 0.05 * jax.random.normal(jax.random.fold_in(_tk, 500 + 0), (125000, 128), jnp.float32)
        tbl_1 = 0.05 * jax.random.normal(jax.random.fold_in(_tk, 500 + 1), (1000, 128), jnp.float32)
        tbl_2 = 0.05 * jax.random.normal(jax.random.fold_in(_tk, 500 + 2), (1250, 128), jnp.float32)
        tbl_3 = 0.05 * jax.random.normal(jax.random.fold_in(_tk, 500 + 3), (1250, 128), jnp.float32)
        tbl_4 = 0.05 * jax.random.normal(jax.random.fold_in(_tk, 500 + 4), (12500, 128), jnp.float32)
        tbl_5 = 0.05 * jax.random.normal(jax.random.fold_in(_tk, 500 + 5), (1000, 128), jnp.float32)
        tbl_6 = 0.05 * jax.random.normal(jax.random.fold_in(_tk, 500 + 6), (12500, 128), jnp.float32)
        tbl_7 = 0.05 * jax.random.normal(jax.random.fold_in(_tk, 500 + 7), (1000, 128), jnp.float32)
        tbl_8 = 0.05 * jax.random.normal(jax.random.fold_in(_tk, 500 + 8), (1000, 128), jnp.float32)
        tbl_9 = 0.05 * jax.random.normal(jax.random.fold_in(_tk, 500 + 9), (1250, 128), jnp.float32)
        tbl_10 = 0.05 * jax.random.normal(jax.random.fold_in(_tk, 500 + 10), (1250, 128), jnp.float32)
        tbl_11 = 0.05 * jax.random.normal(jax.random.fold_in(_tk, 500 + 11), (12500, 128), jnp.float32)
        tbl_12 = 0.05 * jax.random.normal(jax.random.fold_in(_tk, 500 + 12), (12500, 128), jnp.float32)
        tbl_13 = 0.05 * jax.random.normal(jax.random.fold_in(_tk, 500 + 13), (1000, 128), jnp.float32)
        tbl_14 = 0.05 * jax.random.normal(jax.random.fold_in(_tk, 500 + 14), (12500, 128), jnp.float32)
        tbl_15 = 0.05 * jax.random.normal(jax.random.fold_in(_tk, 500 + 15), (12500, 128), jnp.float32)
        tbl_16 = 0.05 * jax.random.normal(jax.random.fold_in(_tk, 500 + 16), (1000, 128), jnp.float32)
        tbl_17 = 0.05 * jax.random.normal(jax.random.fold_in(_tk, 500 + 17), (1250, 128), jnp.float32)
        tbl_18 = 0.05 * jax.random.normal(jax.random.fold_in(_tk, 500 + 18), (1000, 128), jnp.float32)
        tbl_19 = 0.05 * jax.random.normal(jax.random.fold_in(_tk, 500 + 19), (1000, 128), jnp.float32)
        tbl_20 = 0.05 * jax.random.normal(jax.random.fold_in(_tk, 500 + 20), (1000, 128), jnp.float32)
        tbl_21 = 0.05 * jax.random.normal(jax.random.fold_in(_tk, 500 + 21), (1250, 128), jnp.float32)
        tbl_22 = 0.05 * jax.random.normal(jax.random.fold_in(_tk, 500 + 22), (1000, 128), jnp.float32)
        tbl_23 = 0.05 * jax.random.normal(jax.random.fold_in(_tk, 500 + 23), (12500, 128), jnp.float32)
        tbl_24 = 0.05 * jax.random.normal(jax.random.fold_in(_tk, 500 + 24), (1250, 128), jnp.float32)
        tbl_25 = 0.05 * jax.random.normal(jax.random.fold_in(_tk, 500 + 25), (1000, 128), jnp.float32)
        tbl_26 = 0.05 * jax.random.normal(jax.random.fold_in(_tk, 500 + 26), (12500, 128), jnp.float32)
        _rk = jax.random.fold_in(_tk, 7)
        W_top1 = 0.0521996 * jax.random.normal(jax.random.fold_in(_tk, 801), (367, 512), jnp.float32)
        W_top2 = 0.0441942 * jax.random.normal(jax.random.fold_in(_tk, 802), (512, 256), jnp.float32)
        W_top3 = 0.0625 * jax.random.normal(jax.random.fold_in(_tk, 803), (256, 1), jnp.float32)
        b_top1 = jnp.zeros((512,), jnp.float32)
        b_top2 = jnp.zeros((256,), jnp.float32)
        return (dense_ctx, ids, tbl_0, tbl_1, tbl_2, tbl_3, tbl_4, tbl_5, tbl_6, tbl_7, tbl_8, tbl_9, tbl_10, tbl_11, tbl_12, tbl_13, tbl_14, tbl_15, tbl_16, tbl_17, tbl_18, tbl_19, tbl_20, tbl_21, tbl_22, tbl_23, tbl_24, tbl_25, tbl_26, W_top1, b_top1, W_top2, b_top2, W_top3)
    dense_ctx, ids, tbl_0, tbl_1, tbl_2, tbl_3, tbl_4, tbl_5, tbl_6, tbl_7, tbl_8, tbl_9, tbl_10, tbl_11, tbl_12, tbl_13, tbl_14, tbl_15, tbl_16, tbl_17, tbl_18, tbl_19, tbl_20, tbl_21, tbl_22, tbl_23, tbl_24, tbl_25, tbl_26, W_top1, b_top1, W_top2, b_top2, W_top3 = _rec_inputs()

    def _L0_rec_setup():
        import jax, jax.numpy as jnp
        import numpy as np

        def _tri_indices(num_feas):
            return np.array([i * num_feas + j for j in range(1, num_feas) for i in range(j)], dtype=np.int32)
        key = jax.random.key(seed)
        batch, num_feas, embed_dim = (2048, 27, 128)
        inputs = jax.random.normal(key, (batch, num_feas, embed_dim), dtype=jnp.float32)
        return {'inputs': inputs, 'num_feas': num_feas}
    _L0_rec_all = _L0_rec_setup()
    _L0_rec_in = {k: v for k, v in _L0_rec_all.items() if k in ()}
    del _L0_rec_all
    return {'dense_ctx': dense_ctx, 'ids': ids, 'tbl_0': tbl_0, 'tbl_1': tbl_1, 'tbl_2': tbl_2, 'tbl_3': tbl_3, 'tbl_4': tbl_4, 'tbl_5': tbl_5, 'tbl_6': tbl_6, 'tbl_7': tbl_7, 'tbl_8': tbl_8, 'tbl_9': tbl_9, 'tbl_10': tbl_10, 'tbl_11': tbl_11, 'tbl_12': tbl_12, 'tbl_13': tbl_13, 'tbl_14': tbl_14, 'tbl_15': tbl_15, 'tbl_16': tbl_16, 'tbl_17': tbl_17, 'tbl_18': tbl_18, 'tbl_19': tbl_19, 'tbl_20': tbl_20, 'tbl_21': tbl_21, 'tbl_22': tbl_22, 'tbl_23': tbl_23, 'tbl_24': tbl_24, 'tbl_25': tbl_25, 'tbl_26': tbl_26, 'W_top1': W_top1, 'b_top1': b_top1, 'W_top2': W_top2, 'b_top2': b_top2, 'W_top3': W_top3}

def reference(dense_ctx, ids, tbl_0, tbl_1, tbl_2, tbl_3, tbl_4, tbl_5, tbl_6, tbl_7, tbl_8, tbl_9, tbl_10, tbl_11, tbl_12, tbl_13, tbl_14, tbl_15, tbl_16, tbl_17, tbl_18, tbl_19, tbl_20, tbl_21, tbl_22, tbl_23, tbl_24, tbl_25, tbl_26, W_top1, b_top1, W_top2, b_top2, W_top3):
    import jax
    import jax.numpy as jnp

    def _L0_rec_ref(inputs, num_feas):
        import jax, jax.numpy as jnp
        import numpy as np

        def _tri_indices(num_feas):
            return np.array([i * num_feas + j for j in range(1, num_feas) for i in range(j)], dtype=np.int32)
        dot = jnp.einsum('bnd,bmd->bnm', inputs, inputs)
        idx = jnp.asarray(_tri_indices(num_feas))
        flat = dot.reshape(inputs.shape[0], num_feas * num_feas)
        return flat[:, idx]
    e = jnp.stack([tbl_0[ids[:, 0]], tbl_1[ids[:, 1]], tbl_2[ids[:, 2]], tbl_3[ids[:, 3]], tbl_4[ids[:, 4]], tbl_5[ids[:, 5]], tbl_6[ids[:, 6]], tbl_7[ids[:, 7]], tbl_8[ids[:, 8]], tbl_9[ids[:, 9]], tbl_10[ids[:, 10]], tbl_11[ids[:, 11]], tbl_12[ids[:, 12]], tbl_13[ids[:, 13]], tbl_14[ids[:, 14]], tbl_15[ids[:, 15]], tbl_16[ids[:, 16]], tbl_17[ids[:, 17]], tbl_18[ids[:, 18]], tbl_19[ids[:, 19]], tbl_20[ids[:, 20]], tbl_21[ids[:, 21]], tbl_22[ids[:, 22]], tbl_23[ids[:, 23]], tbl_24[ids[:, 24]], tbl_25[ids[:, 25]], tbl_26[ids[:, 26]]], axis=1)
    z = _L0_rec_ref(e, 27)
    z = z.reshape(z.shape[0], -1)
    h = jnp.concatenate([z, dense_ctx], axis=1)
    h = jnp.maximum(h @ W_top1 + b_top1, 0.0)
    h = jnp.maximum(h @ W_top2 + b_top2, 0.0)
    y = h @ W_top3
    return y

_drawn_inputs = setup_inputs


def setup_inputs(seed=0):
    import zlib

    import numpy as np

    out = dict(_drawn_inputs(seed))
    spreads = {'b_top1': (0.0, 0.1), 'b_top2': (0.0, 0.1)}
    factors = {}
    for name, (base, spread) in spreads.items():
        noise = np.random.default_rng([zlib.crc32(name.encode()), seed]).standard_normal(out[name].shape)
        drawn = base * np.exp(spread * noise) if base else spread * noise
        out[name] = jnp.asarray(drawn.astype(out[name].dtype))
    for name, factor in factors.items():
        out[name] = (out[name] * factor).astype(out[name].dtype)
    return out
```

```python
from contextlib import ExitStack

import concourse.bass as bass
from concourse import mybir

F32 = mybir.dt.float32
I32 = mybir.dt.int32
ALU = mybir.AluOpType
ACT = mybir.ActivationFunctionType

P = 128
BATCH, NF, D = 2048, 27, 128
DENSE = 16
H1, H2 = 512, 256
TILES = BATCH // P
PAIRS = TILES // 2
PB = 2 * P
SLOTS = 32
Q = P // SLOTS
J = NF - 1
KT = 7
BANK = 512
GROUP = BANK // P
FGROUPS = [list(range(f, min(f + GROUP, NF))) for f in range(0, NF, GROUP)]
NG = len(FGROUPS)
GPB = BANK // (Q * J)
CB = 2
CHUNKS = P // (Q * GPB * CB)
O1, O2 = H1 // P, H2 // P
DENSE_R, DENSE_T = J // KT, J % KT
LAST_K = SLOTS * (Q - 1)


def build(nc, dense_t, ids, tables, w1, b1, w2, b2, w3, out):
    with ExitStack() as ctx:
        def sb(name, shape, dt=F32):
            return ctx.enter_context(nc.sbuf_tensor(name, shape, dt))

        def psum(name, shape):
            return ctx.enter_context(nc.psum_tensor(name, shape, F32))

        def sem(name):
            return ctx.enter_context(nc.semaphore(name))

        ident = sb("ident", [P, P])
        idx = [sb(f"idx{h}", [P, NF], I32) for h in range(2)]
        e = [sb(f"e{h}", [P, NF, D]) for h in range(2)]
        eT = [sb(f"eT{h}", [P, P, SLOTS]) for h in range(2)]
        z = sb("z", [P, KT, PB])
        w1_sb = sb("w1_sb", [P, KT, H1])
        w2_sb = sb("w2_sb", [P, O1, H2])
        w3_sb = sb("w3_sb", [P, O2])
        b1_sb = sb("b1_sb", [P, O1])
        b2_sb = sb("b2_sb", [P, O2])
        h1 = sb("h1", [P, O1, PB])
        h2 = sb("h2", [P, O2, PB])
        y = sb("y", [1, BATCH])

        tr_ps = [psum(f"tr_ps{n}", [P, GROUP, P]) for n in range(2)]
        gram_ps = [psum(f"gram_ps{n}", [P, CB, BANK]) for n in range(2)]
        mlp_ps = [psum(f"mlp_ps{n}", [P, 2, PB]) for n in range(2)]

        s_w = sem("weights_loaded")
        s_b = sem("biases_loaded")
        s_dense = sem("dense_loaded")
        s_ids = [sem(f"ids{h}_loaded") for h in range(2)]
        s_gath = [[sem(f"gathered{h}_{g}") for g in range(NG)] for h in range(2)]
        s_go = sem("gather_begun")
        s_zero = sem("pads_zeroed")
        s_id0 = sem("ident_zeroed")
        s_ident = sem("ident_ready")
        s_tr = sem("group_transposed")
        s_ev = sem("group_evacuated")
        s_gram = sem("gram_chunk_ready")
        s_ext = sem("gram_chunk_extracted")
        s_l1 = sem("layer1_bank_ready")
        s_h1 = sem("h1_bank_ready")
        s_l2 = sem("layer2_ready")
        s_h2 = sem("h2_ready")
        s_l3 = sem("layer3_ready")
        s_y = sem("y_pair_ready")
        s_out = sem("out_stored")

        dense_rows = z[SLOTS * DENSE_R:SLOTS * DENSE_R + DENSE, DENSE_T, :]

        block = ctx.enter_context(nc.Block())

        @block.sync
        def _(sp):
            def load_ids(h, tile):
                sp.dma_start(idx[h][:, :], ids[bass.ds(tile * P, P), :]).then_inc(s_ids[h], 16)

            load_ids(0, 0)
            load_ids(1, 1)
            sp.wait_ge(s_zero, 3)
            sp.dma_start(dense_rows, dense_t[:, 0:PB]).then_inc(s_dense, 16)
            sp.dma_start(w1_sb[:, :, :], w1).then_inc(s_w, 16)
            sp.dma_start(w2_sb[:, :, :], w2.rearrange("(k p) o -> p k o", p=P)).then_inc(s_w, 16)
            with sp.Fori(1, PAIRS) as i:
                for h in range(2):
                    sp.wait_ge(s_tr, NG * (2 * i - 1 + h))
                    load_ids(h, 2 * i + h)
                sp.wait_ge(s_l1, 2 * i)
                sp.dma_start(dense_rows, dense_t[:, bass.ds(i * PB, PB)]).then_inc(s_dense, 16)
            sp.wait_ge(s_y, PAIRS)
            sp.dma_start(out.rearrange("b o -> o b"), y[:, :]).then_inc(s_out, 16)
            sp.wait_ge(s_out, 16)

        @block.gpsimd
        def _(pool):
            nc.gpsimd.memset(ident[:, :], 0.0).then_inc(s_id0, 1)
            pool.wait_ge(s_id0, 1)
            nc.gpsimd.affine_select(out=ident[:, :], in_=ident[:, :], compare_op=ALU.not_equal, fill=1.0,
                                    base=0, pattern=[[-1, P]], channel_multiplier=1).then_inc(s_ident, 1)

            def gather_tile(h, i):
                pool.wait_ge(s_ids[h], 16 * (i + 1))
                nc.gpsimd.sem_inc(s_go, 1)
                for g, group in enumerate(FGROUPS):
                    for f in group:
                        pool.indirect_dma_start(
                            out=e[h][:, f, :], out_offset=None, in_=tables[f],
                            in_offset=bass.IndirectOffsetOnAxis(ap=idx[h][:, f:f + 1], axis=0),
                        ).then_inc(s_gath[h][g], 16)

            gather_tile(0, 0)
            gather_tile(1, 0)
            with pool.Fori(1, PAIRS) as i:
                gather_tile(0, i)
                gather_tile(1, i)

        @block.tensor
        def _(pe):
            def transpose_tile(h, i, first):
                for g, group in enumerate(FGROUPS):
                    n = NG * h + g
                    pe.wait_ge(s_gath[h][g], 16 * len(group) * (i + 1))
                    if not (first and n < 2):
                        pe.wait_ge(s_ev, 2 * NG * i + n - 1)
                    for k, f in enumerate(group):
                        last = nc.tensor.transpose(tr_ps[n % 2][:, k, :], e[h][:, f, :], ident[:, :])
                    last.then_inc(s_tr, 1)

            def gram_tile(h, i, first):
                pe.wait_ge(s_ev, NG * (2 * i + h + 1))
                for c in range(CHUNKS):
                    n = CHUNKS * h + c
                    if not (first and n < 2):
                        pe.wait_ge(s_ext, 2 * CHUNKS * i + n - 1)
                    for k in range(CB * GPB):
                        b = (c * CB * GPB + k) * Q
                        col = (k % GPB) * Q * J
                        last = nc.tensor.matmul(
                            gram_ps[n % 2][:, k // GPB, col:col + Q * J],
                            eT[h][:, b:b + Q, :],
                            eT[h][:, b:b + Q, 1:NF], start=True, stop=True)
                    last.then_inc(s_gram, 1)

            def mlp_pair(i, first):
                pe.wait_ge(s_ext, 2 * CHUNKS * (i + 1))
                pe.wait_ge(s_dense, 16 * (i + 1))
                if not first:
                    pe.wait_ge(s_h2, i)
                    pe.wait_ge(s_y, i)
                for o in range(O1):
                    for k in range(KT):
                        rows = P if k < KT - 1 else LAST_K
                        last = nc.tensor.matmul(mlp_ps[o // 2][:, o % 2, :],
                                                w1_sb[0:rows, k, o * P:(o + 1) * P], z[0:rows, k, :],
                                                start=(k == 0), stop=(k == KT - 1))
                    if o % 2:
                        last.then_inc(s_l1, 1)
                pe.wait_ge(s_h1, 2 * (i + 1))
                for o in range(O2):
                    for k in range(O1):
                        last = nc.tensor.matmul(mlp_ps[0][:, o, :], w2_sb[:, k, o * P:(o + 1) * P],
                                                h1[:, k, :], start=(k == 0), stop=(k == O1 - 1))
                last.then_inc(s_l2, 1)
                pe.wait_ge(s_h2, i + 1)
                for k in range(O2):
                    last = nc.tensor.matmul(mlp_ps[1][0:1, 0, :], w3_sb[:, k:k + 1], h2[:, k, :],
                                            start=(k == 0), stop=(k == O2 - 1))
                last.then_inc(s_l3, 1)

            pe.wait_ge(s_ident, 1)
            pe.wait_ge(s_zero, 3)
            for h in range(2):
                transpose_tile(h, 0, True)
                gram_tile(h, 0, True)
            pe.wait_ge(s_w, 2 * 16)
            pe.wait_ge(s_b, 3 * 16)
            mlp_pair(0, True)
            with pe.Fori(1, PAIRS) as i:
                for h in range(2):
                    transpose_tile(h, i, False)
                    gram_tile(h, i, False)
                mlp_pair(i, False)

        @block.scalar
        def _(act):
            act.dma_start(b1_sb[:, :], b1).then_inc(s_b, 16)
            act.dma_start(b2_sb[:, :], b2).then_inc(s_b, 16)
            act.dma_start(w3_sb[:, :], w3).then_inc(s_b, 16)

            def evacuate_tile(h, i, first):
                if not first:
                    act.wait_ge(s_gram, CHUNKS * (2 * i + h - 1))
                for g, group in enumerate(FGROUPS):
                    n = NG * h + g
                    act.wait_ge(s_tr, 2 * NG * i + n + 1)
                    f = group[0]
                    nc.scalar.copy(eT[h][:, :, f:f + len(group)].rearrange("d b f -> d f b"),
                                   tr_ps[n % 2][:, 0:len(group), :]).then_inc(s_ev, 1)

            def relu_pair(i):
                for m in range(2):
                    act.wait_ge(s_l1, 2 * i + m + 1)
                    for o in range(2 * m, 2 * m + 2):
                        last = nc.scalar.activation(h1[:, o, :], mlp_ps[m][:, o % 2, :], ACT.Relu,
                                                    bias=b1_sb[:, o:o + 1])
                    last.then_inc(s_h1, 1)
                act.wait_ge(s_l2, i + 1)
                for o in range(O2):
                    last = nc.scalar.activation(h2[:, o, :], mlp_ps[0][:, o, :], ACT.Relu,
                                                bias=b2_sb[:, o:o + 1])
                last.then_inc(s_h2, 1)
                act.wait_ge(s_l3, i + 1)
                nc.scalar.copy(y[:, bass.ds(i * PB, PB)], mlp_ps[1][0:1, 0, :]).then_inc(s_y, 1)

            evacuate_tile(0, 0, True)
            evacuate_tile(1, 0, True)
            act.wait_ge(s_b, 3 * 16)
            relu_pair(0)
            with act.Fori(1, PAIRS) as i:
                evacuate_tile(0, i, False)
                evacuate_tile(1, i, False)
                relu_pair(i)

        @block.vector
        def _(dve):
            for h in range(2):
                nc.vector.memset(eT[h][:, :, NF:SLOTS], 0.0).then_inc(s_zero, 1)
            nc.vector.memset(z[:, :, :], 0.0).then_inc(s_zero, 1)

            def extract_tile(h, i):
                for c in range(CHUNKS):
                    n = CHUNKS * h + c
                    dve.wait_ge(s_gram, 2 * CHUNKS * i + n + 1)
                    b0 = h * P + c * CB * GPB * Q
                    samples = z[:, :, b0:b0 + CB * GPB * Q].rearrange("p k (a g q) -> p a g q k", a=CB, q=Q)
                    grams = gram_ps[n % 2][:, :, 0:GPB * Q * J].rearrange("p a (g q j) -> p a g q j", g=GPB, q=Q)
                    for q in range(Q):
                        for r in range(Q):
                            nk = min(KT, J - KT * r)
                            last = nc.vector.tensor_copy(
                                samples[SLOTS * r:SLOTS * (r + 1), :, :, q, 0:nk],
                                grams[SLOTS * q:SLOTS * (q + 1), :, :, q, KT * r:KT * r + nk])
                    last.then_inc(s_ext, 1)

            dve.wait_ge(s_zero, 3)
            extract_tile(0, 0)
            extract_tile(1, 0)
            with dve.Fori(1, PAIRS) as i:
                dve.wait_ge(s_l1, 2 * i)
                extract_tile(0, i)
                extract_tile(1, i)


def kernel(**inputs):
    import numpy as np
    import concourse.bacc as bacc
    from concourse.bass_utils import run_bass_kernel_spmd

    nc = bacc.Bacc("TRN2", target_bir_lowering=False, num_devices=1)
    arrays = {}

    def dram(name, a):
        a = np.ascontiguousarray(a)
        arrays[name] = a
        return nc.dram_tensor(name, a.shape, mybir.dt.from_np(a.dtype), kind="ExternalInput").ap()

    w = np.asarray(inputs["W_top1"])
    w1 = np.zeros((P, KT, H1), w.dtype)
    for k in range(J):
        j, r, t = k + 1, k // KT, k % KT
        w1[SLOTS * r:SLOTS * r + j, t] = w[j * (j - 1) // 2:j * (j + 1) // 2]
    w1[SLOTS * DENSE_R:SLOTS * DENSE_R + DENSE, DENSE_T] = w[NF * J // 2:]

    args = [
        dram("dense_t", np.asarray(inputs["dense_ctx"]).T),
        dram("ids", inputs["ids"]),
        [dram(f"tbl_{f}", inputs[f"tbl_{f}"]) for f in range(NF)],
        dram("w1", w1),
        dram("b1", np.asarray(inputs["b_top1"]).reshape(O1, P).T),
        dram("w2", inputs["W_top2"]),
        dram("b2", np.asarray(inputs["b_top2"]).reshape(O2, P).T),
        dram("w3", np.asarray(inputs["W_top3"]).reshape(O2, P).T),
    ]
    out = nc.dram_tensor("out", (BATCH, 1), F32, kind="ExternalOutput").ap()
    build(nc, *args, out)
    r = run_bass_kernel_spmd(nc, [arrays], core_ids=[0])
    return r.results[0]["out"]
```

```python
from contextlib import ExitStack

import concourse.bass as bass
from concourse import mybir

F32 = mybir.dt.float32
F32R = mybir.dt.float32r
I32 = mybir.dt.int32
ALU = mybir.AluOpType
ACT = mybir.ActivationFunctionType

P = 128
BATCH, NF, D = 2048, 27, 128
DENSE = 16
H1, H2 = 512, 256
ROWS = 1000
ONEHOT = [1, 5, 7, 8, 13, 16]
GATHERED = [f for f in range(NF) if f not in ONEHOT]
FEATURE = GATHERED + ONEHOT
TILES = BATCH // P
PAIRS = TILES // 2
PB = 2 * P
SLOTS = 32
Q = P // SLOTS
GW = (Q - 1) * SLOTS + NF
HALF = NF // 2
NB = HALF + 1
KT = -(-NB // Q)
BANK = 512
GPB = BANK // P
CB = 2
CHUNKS = P // (Q * GPB * CB)
O1, O2 = H1 // P, H2 // P
LAST_R, LAST_T = HALF // KT, HALF % KT
DENSE_P = SLOTS * LAST_R + HALF

NX, NGATH = len(ONEHOT), len(GATHERED)
RT = -(-ROWS // P)
GROUP = 3
GROUPS = [list(range(s, min(s + GROUP, NGATH))) for s in range(0, NGATH, GROUP)]
NG = len(GROUPS)


def ring_order():
    order = []
    for g in range(max(NG, NX)):
        order += [("A", g)] * (g < NG) + [("X", g)] * (g < NX)
    return order + [("B", g) for g in range(NG)]


def k_rows(t):
    return P if t <= LAST_T else SLOTS * LAST_R


RING = ring_order()
SELECTS = 2
EARLY = 1
NR = len(RING)
A_END = NR - NG
assert NGATH % GROUP == 0
assert NR % 2 == 0 and NX % 2 == 0


def build(nc, dense_t, ids, ids_t, low_half, tables, w1, b1, w2, b2, w3, out):
    with ExitStack() as ctx:
        def sb(name, shape, dt=F32):
            return ctx.enter_context(nc.sbuf_tensor(name, shape, dt))

        def psum(name, shape):
            return ctx.enter_context(nc.psum_tensor(name, shape, F32))

        def sem(name):
            return ctx.enter_context(nc.semaphore(name))

        ident = sb("ident", [P, P])
        idx = [sb(f"idx{h}", [P, NF], I32) for h in range(2)]
        e = [sb(f"e{h}", [P, NGATH, D]) for h in range(2)]
        eT = sb("eT", [P, 2, P, SLOTS])
        row_i = sb("row_i", [P, RT], I32)
        row_f = sb("row_f", [P, RT])
        ids_x = sb("ids_x", [P, NX, PB], I32)
        raw = [sb(f"raw{n}", [P, RT, D]) for n in range(2)]
        hi = sb("hi", [P, NX, RT, D], F32R)
        lo = sb("lo", [P, NX, RT, D], F32R)
        oh = [sb(f"oh{n}", [P, RT, PB], F32R) for n in range(2)]
        z = sb("z", [P, 2, KT, PB])
        from_low = sb("from_low", [P, KT], I32)
        w1_sb = sb("w1_sb", [P, KT, H1])
        w2_sb = sb("w2_sb", [P, O1, H2])
        w3_sb = sb("w3_sb", [P, O2])
        b1_sb = sb("b1_sb", [P, O1])
        b2_sb = sb("b2_sb", [P, O2])
        h1 = sb("h1", [P, O1, PB])
        h2 = sb("h2", [P, O2, PB])
        y = sb("y", [1, P + BATCH])

        ring_ps = [psum(f"ring_ps{n}", [P, BANK // P, P]) for n in range(2)]
        gram_ps = [psum(f"gram_ps{n}", [P, CB, BANK]) for n in range(2)]
        mlp_ps = [psum(f"mlp_ps{n}", [P, 2, PB]) for n in range(2)]

        s_w = sem("weights_loaded")
        s_b = sem("biases_loaded")
        s_raw = [sem(f"raw{n}_loaded") for n in range(2)]
        s_split = sem("table_split")
        s_hi = sem("table_high_part")
        s_dense = sem("dense_loaded")
        s_ids = [sem(f"ids{h}_loaded") for h in range(2)]
        s_idx = sem("ids_x_loaded")
        s_gath = [[sem(f"gathered{h}_{g}") for g in range(NG)] for h in range(2)]
        s_go = sem("gather_begun")
        s_zero = sem("pads_zeroed")
        s_id0 = sem("ident_zeroed")
        s_ident = sem("ident_ready")
        s_row = sem("row_numbers")
        s_rowf = sem("row_numbers_float")
        s_oh = sem("onehot_ready")
        s_ring = sem("ring_bank_filled")
        s_ev = sem("ring_bank_evacuated")
        s_gram = sem("gram_chunk_ready")
        s_extv = sem("gram_chunk_extracted_by_vector")
        s_exta = sem("gram_chunk_extracted_by_scalar")
        s_vgo = sem("selection_begun")
        s_mask = sem("mask_loaded")
        s_sel = sem("z_part_selected")
        s_l1 = sem("layer1_bank_ready")
        s_h1 = sem("h1_bank_ready")
        s_l2 = sem("layer2_ready")
        s_h2 = sem("h2_ready")
        s_l3 = sem("layer3_ready")
        s_y = sem("y_ready")
        s_out = sem("out_stored")

        zin = z[:, 1]
        dense_rows = zin[DENSE_P:DENSE_P + DENSE, LAST_T, :]

        def rows_of(k):
            return min(P, ROWS - k * P)

        def place(h):
            return P * (1 - h)

        def extract(copy, quads, c, h):
            n = CHUNKS * h + c
            b0 = place(h) + c * CB * GPB * Q
            samples = z[:, :, :, b0:b0 + CB * GPB * Q].rearrange("p v t (g q) -> p q g v t", q=Q)
            products = gram_ps[n % 2][:, :, :].rearrange("p a (g c) -> p (a g) c", c=P)
            for q in quads:
                own = products[SLOTS * q:SLOTS * q + NF, :, q * NF:(q + 1) * NF]
                for r in range(LAST_R + 1):
                    nt = min(KT, HALF - KT * r)
                    pairs = bass.AP(own.tensor, own.offset + KT * r,
                                    [list(own.ap[0]), list(own.ap[1]), [HALF + 1, 2], [1, nt]])
                    copy(samples[SLOTS * r:SLOTS * r + NF, q, :, :, 0:nt], pairs)
                last = copy(samples[SLOTS * LAST_R:SLOTS * LAST_R + HALF, q, :, 1, LAST_T],
                            products[SLOTS * q:SLOTS * q + HALF, :, q * NF + HALF])
            return last

        block = ctx.enter_context(nc.Block())

        @block.sync
        def _(sp):
            def load_ids(h, tile):
                sp.dma_start(idx[h][:, :], ids[bass.ds(tile * P, P), :]).then_inc(s_ids[h], 16)

            def gathers_done(h, i):
                for g in range(NG):
                    sp.wait_ge(s_gath[h][g], 16 * GROUP * (i + 1))

            def load_ids_x(i):
                sp.dma_start(ids_x[:, :, :], ids_t[:, bass.ds(i * PB, PB)].partition_broadcast(P)).then_inc(s_idx, 16)

            load_ids(0, 0)
            load_ids(1, 1)
            load_ids_x(0)
            sp.dma_start(from_low[:, :], low_half).then_inc(s_mask, 16)
            for u, f in enumerate(ONEHOT):
                if u >= 2:
                    sp.wait_ge(s_split, u - 1)
                full = ROWS // P
                sp.dma_start(raw[u % 2][:, 0:full, :],
                             tables[f][0:full * P, :].rearrange("(k p) d -> p k d", p=P)).then_inc(s_raw[u % 2], 16)
                sp.dma_start(raw[u % 2][0:ROWS - full * P, full, :],
                             tables[f][full * P:ROWS, :]).then_inc(s_raw[u % 2], 16)
            sp.wait_ge(s_zero, 2)
            sp.dma_start(dense_rows[:, P:PB], dense_t[:, 0:P]).then_inc(s_dense, 16)
            with sp.Fori(1, PAIRS) as i:
                gathers_done(0, i - 1)
                load_ids(0, 2 * i)
                sp.wait_ge(s_oh, NX * i)
                load_ids_x(i)
                gathers_done(1, i - 1)
                load_ids(1, 2 * i + 1)
                sp.wait_ge(s_l1, 2 * i)
                sp.dma_start(dense_rows, dense_t[:, bass.ds(i * PB - P, PB)]).then_inc(s_dense, 16)
            sp.wait_ge(s_l1, 2 * PAIRS)
            sp.dma_start(dense_rows[:, 0:P], dense_t[:, BATCH - P:BATCH]).then_inc(s_dense, 16)
            sp.wait_ge(s_y, PAIRS + 1)
            sp.dma_start(out.rearrange("b o -> o b"), y[:, P:P + BATCH]).then_inc(s_out, 16)
            sp.wait_ge(s_out, 16)

        @block.gpsimd
        def _(pool):
            def gather_tile(h, i, first=False):
                pool.wait_ge(s_ids[h], 16 * (i + 1))
                nc.gpsimd.sem_inc(s_go, 1)
                for g, group in enumerate(GROUPS):
                    if not first:
                        pool.wait_ge(s_ring, NR * (i - 1) + RING.index(("AB"[h], g)) + 1)
                        nc.gpsimd.sem_inc(s_go, 1)
                    for s in group:
                        f = FEATURE[s]
                        pool.indirect_dma_start(
                            out=e[h][:, s, :], out_offset=None, in_=tables[f],
                            in_offset=bass.IndirectOffsetOnAxis(ap=idx[h][:, f:f + 1], axis=0),
                        ).then_inc(s_gath[h][g], 16)

            nc.gpsimd.memset(ident[:, :], 0.0).then_inc(s_id0, 1)
            nc.gpsimd.iota(row_i[:, :], pattern=[[P, RT]], base=0, channel_multiplier=1).then_inc(s_row, 1)
            pool.wait_ge(s_id0, 1)
            nc.gpsimd.affine_select(out=ident[:, :], in_=ident[:, :], compare_op=ALU.not_equal, fill=1.0,
                                    base=0, pattern=[[-1, P]], channel_multiplier=1).then_inc(s_ident, 1)
            gather_tile(0, 0, True)
            gather_tile(1, 0, True)
            with pool.Fori(1, PAIRS) as i:
                gather_tile(0, i)
                gather_tile(1, i)

        @block.tensor
        def _(pe):
            def fill(n, i, first):
                kind, g = RING[n]
                if not (first and n < 2):
                    pe.wait_ge(s_ev, NR * i + n - 1)
                if kind == "X":
                    pe.wait_ge(s_oh, NX * i + g + 1)
                    for k in range(RT):
                        rows = rows_of(k)
                        for part in (hi, lo):
                            last = nc.tensor.matmul(
                                ring_ps[n % 2][:, 0:2, :].rearrange("d a b -> d (a b)"),
                                part[0:rows, g, k, :], oh[g % 2][0:rows, k, :],
                                start=(k == 0 and part is hi), stop=(k == RT - 1 and part is lo))
                else:
                    h = "AB".index(kind)
                    pe.wait_ge(s_gath[h][g], 16 * len(GROUPS[g]) * (i + 1))
                    for k, s in enumerate(GROUPS[g]):
                        last = nc.tensor.transpose(ring_ps[n % 2][:, k, :], e[h][:, s, :], ident[:, :])
                last.then_inc(s_ring, 1)

            def gram_tile(h, i, first=False):
                pe.wait_ge(s_ev, NR * i + (A_END if h == 0 else NR))
                for c in range(CHUNKS):
                    n = CHUNKS * h + c
                    if not (first and n < 2):
                        pe.wait_ge(s_extv, 2 * CHUNKS * i + n - 1)
                        pe.wait_ge(s_exta, 2 * CHUNKS * i + n - 1)
                    for k in range(CB * GPB):
                        b = (c * CB * GPB + k) * Q
                        col = (k % GPB) * P
                        slots = eT[:, h, b:b + Q, :].rearrange("d q s -> d (q s)")[:, 0:GW]
                        last = nc.tensor.matmul(gram_ps[n % 2][0:GW, k // GPB, col:col + Q * NF], slots,
                                                eT[:, h, b:b + Q, 0:NF], start=True, stop=True)
                    last.then_inc(s_gram, 1)

            def layer1(m, half, cols):
                for o in range(2 * half, 2 * half + 2):
                    for t in range(KT):
                        last = nc.tensor.matmul(mlp_ps[half][:, o % 2, cols],
                                                w1_sb[0:k_rows(t), t, o * P:(o + 1) * P],
                                                zin[0:k_rows(t), t, cols],
                                                start=(t == 0), stop=(t == KT - 1))
                last.then_inc(s_l1, 1)

            def layer2(m, cols):
                pe.wait_ge(s_h1, 2 * (m + 1))
                for o in range(O2):
                    for k in range(O1):
                        last = nc.tensor.matmul(mlp_ps[0][:, o, cols], w2_sb[:, k, o * P:(o + 1) * P],
                                                h1[:, k, cols], start=(k == 0), stop=(k == O1 - 1))
                last.then_inc(s_l2, 1)

            def layer3(m, cols):
                pe.wait_ge(s_h2, m + 1)
                for k in range(O2):
                    last = nc.tensor.matmul(mlp_ps[1][0:1, 0, cols], w3_sb[:, k:k + 1], h2[:, k, cols],
                                            start=(k == 0), stop=(k == O2 - 1))
                last.then_inc(s_l3, 1)

            def step_b(i, first=False):
                cols = slice(0, PB)
                for g in range(EARLY):
                    fill(A_END + g, i, False)
                pe.wait_ge(s_sel, SELECTS * (2 * i + 1))
                pe.wait_ge(s_dense, 16 * (i + 1))
                if not first:
                    pe.wait_ge(s_h2, i)
                layer1(i, 0, cols)
                if not first:
                    pe.wait_ge(s_y, i)
                layer1(i, 1, cols)
                for g in range(EARLY, NG):
                    fill(A_END + g, i, False)
                layer2(i, cols)

            pe.wait_ge(s_ident, 1)
            for n in range(A_END):
                fill(n, 0, True)
            pe.wait_ge(s_zero, 2)
            gram_tile(0, 0, True)
            pe.wait_ge(s_w, 2 * 16)
            pe.wait_ge(s_b, 3 * 16)
            step_b(0, True)
            with pe.Fori(1, PAIRS) as i:
                gram_tile(1, i - 1)
                for n in range(A_END):
                    fill(n, i, False)
                layer3(i - 1, slice(0, PB))
                gram_tile(0, i)
                step_b(i)
            gram_tile(1, PAIRS - 1)
            layer3(PAIRS - 1, slice(0, PB))
            tail = slice(0, P)
            pe.wait_ge(s_sel, SELECTS * TILES)
            pe.wait_ge(s_dense, 16 * (PAIRS + 1))
            layer1(PAIRS, 0, tail)
            pe.wait_ge(s_y, PAIRS)
            layer1(PAIRS, 1, tail)
            layer2(PAIRS, tail)
            layer3(PAIRS, tail)

        @block.scalar
        def _(act):
            def evacuate(n, i):
                kind, g = RING[n]
                act.wait_ge(s_ring, NR * i + n + 1)
                if kind == "X":
                    nc.scalar.copy(eT[:, :, :, NGATH + g], ring_ps[n % 2][:, 0:2, :]).then_inc(s_ev, 1)
                else:
                    h, s, ns = "AB".index(kind), GROUPS[g][0], len(GROUPS[g])
                    nc.scalar.copy(eT[:, h, :, s:s + ns].rearrange("d b s -> d s b"),
                                   ring_ps[n % 2][:, 0:ns, :]).then_inc(s_ev, 1)

            def extract_tile(h, i):
                for c in range(CHUNKS):
                    act.wait_ge(s_gram, CHUNKS * (2 * i + h) + c + 1)
                    extract(nc.scalar.copy, (2, 3), c, h).then_inc(s_exta, 1)

            def relu1(m, half, cols):
                act.wait_ge(s_l1, 2 * m + half + 1)
                for o in range(2 * half, 2 * half + 2):
                    last = nc.scalar.activation(h1[:, o, cols], mlp_ps[half][:, o % 2, cols], ACT.Relu,
                                                bias=b1_sb[:, o:o + 1])
                last.then_inc(s_h1, 1)

            def relu2(m, cols):
                act.wait_ge(s_l2, m + 1)
                for o in range(O2):
                    last = nc.scalar.activation(h2[:, o, cols], mlp_ps[0][:, o, cols], ACT.Relu,
                                                bias=b2_sb[:, o:o + 1])
                last.then_inc(s_h2, 1)

            def output(m, samples, cols):
                act.wait_ge(s_l3, m + 1)
                nc.scalar.copy(y[:, samples], mlp_ps[1][0:1, 0, cols]).then_inc(s_y, 1)

            def step_b(i):
                cols = slice(0, PB)
                for g in range(EARLY):
                    evacuate(A_END + g, i)
                relu1(i, 0, cols)
                relu1(i, 1, cols)
                for g in range(EARLY, NG):
                    evacuate(A_END + g, i)
                relu2(i, cols)

            act.dma_start(b1_sb[:, :], b1).then_inc(s_b, 16)
            act.dma_start(b2_sb[:, :], b2).then_inc(s_b, 16)
            act.dma_start(w3_sb[:, :], w3).then_inc(s_b, 16)
            act.dma_start(w1_sb[:, :, :], w1).then_inc(s_w, 16)
            act.dma_start(w2_sb[:, :, :], w2.rearrange("(k p) o -> p k o", p=P)).then_inc(s_w, 16)
            for n in range(A_END):
                evacuate(n, 0)
            act.wait_ge(s_zero, 2)
            extract_tile(0, 0)
            act.wait_ge(s_b, 3 * 16)
            step_b(0)
            with act.Fori(1, PAIRS) as i:
                act.wait_ge(s_l1, 2 * i)
                extract_tile(1, i - 1)
                for n in range(A_END):
                    evacuate(n, i)
                output(i - 1, bass.ds((i - 1) * PB, PB), slice(0, PB))
                extract_tile(0, i)
                step_b(i)
            tail = slice(0, P)
            act.wait_ge(s_l1, 2 * PAIRS)
            extract_tile(1, PAIRS - 1)
            output(PAIRS - 1, slice(BATCH - PB, BATCH), slice(0, PB))
            relu1(PAIRS, 0, tail)
            relu1(PAIRS, 1, tail)
            relu2(PAIRS, tail)
            output(PAIRS, slice(BATCH, BATCH + P), tail)

        @block.vector
        def _(dve):
            def onehot(u, i):
                for k in range(RT):
                    last = nc.vector.tensor_scalar(oh[u % 2][0:rows_of(k), k, :], ids_x[0:rows_of(k), u, :],
                                                   row_f[0:rows_of(k), k:k + 1], None, ALU.is_equal)
                last.then_inc(s_oh, 1)

            def onehots(us, i, first=False):
                for u in us:
                    if u >= 2:
                        dve.wait_ge(s_ring, NR * i + RING.index(("X", u - 2)) + 1)
                    elif not first:
                        dve.wait_ge(s_ring, NR * (i - 1) + RING.index(("X", NX + u - 2)) + 1)
                    onehot(u, i)

            def extract_tile(h, i):
                for c in range(CHUNKS):
                    dve.wait_ge(s_gram, CHUNKS * (2 * i + h) + c + 1)
                    extract(nc.vector.tensor_copy, (0, 1), c, h).then_inc(s_extv, 1)
                    if (c + 1) % (CHUNKS // SELECTS) == 0:
                        select(h, i, c)

            def select(h, i, c):
                dve.wait_ge(s_extv, CHUNKS * (2 * i + h) + c + 1)
                dve.wait_ge(s_exta, CHUNKS * (2 * i + h) + c + 1)
                nc.vector.sem_inc(s_vgo, 1)
                nb = P // SELECTS
                b0 = place(h) + (c + 1) * P // CHUNKS - nb
                for rows, nt in ((slice(0, SLOTS * LAST_R), KT), (slice(SLOTS * LAST_R, P), LAST_T)):
                    last = nc.vector.copy_predicated(
                        z[rows, 1, 0:nt, b0:b0 + nb],
                        from_low[rows, 0:nt].rearrange("p (t b) -> p t b", b=1).to_broadcast([rows.stop - rows.start, nt, nb]),
                        z[rows, 0, 0:nt, b0:b0 + nb])
                last.then_inc(s_sel, 1)

            dve.wait_ge(s_row, 1)
            nc.vector.tensor_copy(row_f[:, :], row_i[:, :]).then_inc(s_rowf, 1)
            nc.vector.memset(eT[:, :, :, NF:SLOTS], 0.0).then_inc(s_zero, 1)
            nc.vector.memset(z[:, :, :, :], 0.0).then_inc(s_zero, 1)

            def split(u):
                dve.wait_ge(s_raw[u % 2], 32 * (u // 2 + 1))
                full = ROWS // P
                for n, (rows, tiles) in enumerate([(P, slice(0, full)), (ROWS - full * P, slice(full, RT))]):
                    nc.vector.tensor_copy(hi[0:rows, u, tiles, :], raw[u % 2][0:rows, tiles, :]).then_inc(s_hi, 1)
                for n, (rows, tiles) in enumerate([(P, slice(0, full)), (ROWS - full * P, slice(full, RT))]):
                    dve.wait_ge(s_hi, 2 * u + n + 1)
                    last = nc.vector.tensor_tensor(lo[0:rows, u, tiles, :], raw[u % 2][0:rows, tiles, :],
                                                   hi[0:rows, u, tiles, :].bitcast(F32), ALU.subtract)
                last.then_inc(s_split, 1)

            dve.wait_ge(s_rowf, 1)
            dve.wait_ge(s_idx, 16)
            for u in range(NX):
                split(u)
                onehots([u], 0, True)
            dve.wait_ge(s_zero, 2)
            dve.wait_ge(s_mask, 16)
            extract_tile(0, 0)
            with dve.Fori(1, PAIRS) as i:
                dve.wait_ge(s_idx, 16 * (i + 1))
                onehots(range(2), i)
                dve.wait_ge(s_l1, 2 * i)
                extract_tile(1, i - 1)
                onehots(range(2, NX), i)
                extract_tile(0, i)
            dve.wait_ge(s_l1, 2 * PAIRS)
            extract_tile(1, PAIRS - 1)


def kernel(**inputs):
    import numpy as np
    import concourse.bacc as bacc
    from concourse.bass_utils import run_bass_kernel_spmd

    nc = bacc.Bacc("TRN2", target_bir_lowering=False, num_devices=1)
    arrays = {}

    def dram(name, a):
        a = np.ascontiguousarray(a)
        arrays[name] = a
        return nc.dram_tensor(name, a.shape, mybir.dt.from_np(a.dtype), kind="ExternalInput").ap()

    w = np.asarray(inputs["W_top1"])
    def pair(a, b):
        fi, fj = sorted((FEATURE[a], FEATURE[b]))
        return w[fj * (fj - 1) // 2 + fi]

    w1 = np.zeros((P, KT, H1), w.dtype)
    low_half = np.zeros((P, KT), np.int32)
    for n in range(HALF):
        for i in range(NF):
            p, t = SLOTS * (n // KT) + i, n % KT
            low_half[p, t] = not n <= i <= n + HALF
            if i != n:
                w1[p, t] = pair(i, n if low_half[p, t] else n + HALF + 1)
    for i in range(HALF):
        w1[SLOTS * LAST_R + i, LAST_T] = pair(i, HALF)
    w1[DENSE_P:DENSE_P + DENSE, LAST_T] = w[NF * (NF - 1) // 2:]

    args = [
        dram("dense_t", np.asarray(inputs["dense_ctx"]).T),
        dram("ids", inputs["ids"]),
        dram("ids_t", np.asarray(inputs["ids"])[:, ONEHOT].T),
        dram("low_half", low_half),
        [dram(f"tbl_{f}", inputs[f"tbl_{f}"]) for f in range(NF)],
        dram("w1", w1),
        dram("b1", np.asarray(inputs["b_top1"]).reshape(O1, P).T),
        dram("w2", inputs["W_top2"]),
        dram("b2", np.asarray(inputs["b_top2"]).reshape(O2, P).T),
        dram("w3", np.asarray(inputs["W_top3"]).reshape(O2, P).T),
    ]
    out = nc.dram_tensor("out", (BATCH, 1), F32, kind="ExternalOutput").ap()
    build(nc, *args, out)
    r = run_bass_kernel_spmd(nc, [arrays], core_ids=[0])
    return r.results[0]["out"]
```

```python
from contextlib import ExitStack

import concourse.bass as bass
from concourse import mybir

F32 = mybir.dt.float32
F32R = mybir.dt.float32r
I32 = mybir.dt.int32
ALU = mybir.AluOpType
ACT = mybir.ActivationFunctionType

P = 128
BATCH, NF, D = 2048, 27, 128
DENSE = 16
H1, H2 = 512, 256
ROWS = 1000
ONEHOT = [1, 5, 7, 8, 13, 16, 18, 19]
GATHERED = [f for f in range(NF) if f not in ONEHOT]
FEATURE = GATHERED + ONEHOT
TILES = BATCH // P
PAIRS = TILES // 2
PB = 2 * P
SLOTS = 32
Q = P // SLOTS
GW = (Q - 1) * SLOTS + NF
HALF = NF // 2
NB = HALF + 1
KT = -(-NB // Q)
BANK = 512
GPB = BANK // P
CB = 2
CHUNKS = P // (Q * GPB * CB)
O1, O2 = H1 // P, H2 // P
LAST_R, LAST_T = HALF // KT, HALF % KT
DENSE_P = SLOTS * LAST_R + HALF

RB = 4
VQ = 1
AHEAD = 2
EARLY = (2, 5)
NX, NGATH = len(ONEHOT), len(GATHERED)
RT = -(-ROWS // P)
NSPLIT = NX + 3
GROUP = 3
NG = NGATH // GROUP
GROUPS = [list(range(GROUP * g, GROUP * (g + 1) if g < NG - 1 else NGATH)) for g in range(NG)]
OHB = 3


def ring_order():
    order = []
    for u in range(NX):
        g = u - (NX - NG)
        order += [("A", g)] * (g >= 0) + [("X", u)]
    return order + [("B", g) for g in range(NG)]


def last_use(n, count, buffers):
    if n >= buffers:
        return n - buffers, 0
    return max(m for m in range(count) if m % buffers == n), 1


def k_rows(t):
    return P if t <= LAST_T else SLOTS * LAST_R


RING = ring_order()
NR = len(RING)
assert NG <= NX and 2 * GROUP > NGATH - GROUP * (NG - 1) and NGATH - GROUP * (NG - 1) <= BANK // P
A_END = NR - NG


def build(nc, dense_t, ids, ids_t, low_half, tables, w1, b1, w2, b2, w3, out):
    with ExitStack() as ctx:
        def sb(name, shape, dt=F32):
            return ctx.enter_context(nc.sbuf_tensor(name, shape, dt))

        def psum(name, shape):
            return ctx.enter_context(nc.psum_tensor(name, shape, F32))

        def sem(name):
            return ctx.enter_context(nc.semaphore(name))

        ident = sb("ident", [P, P])
        idx = [sb(f"idx{h}", [P, NF], I32) for h in range(2)]
        e = [sb(f"e{h}", [P, NGATH, D]) for h in range(2)]
        eT = sb("eT", [P, 2, P, SLOTS])
        row_i = sb("row_i", [P, RT], I32)
        row_f = sb("row_f", [P, RT])
        ids_x = sb("ids_x", [P, NX, PB], I32)
        raw = [sb(f"raw{n}", [P, RT, D]) for n in range(2)]
        hi = sb("hi", [P, NX, RT, D], F32R)
        lo = sb("lo", [P, NX, RT, D], F32R)
        oh = [sb(f"oh{n}", [P, RT, PB], F32R) for n in range(OHB)]
        z = sb("z", [P, 2, KT, PB])
        z_hi, z_lo = [sb(f"z_{part}", [P, KT, PB], F32R) for part in ("hi", "lo")]
        from_low = sb("from_low", [P, KT], I32)
        w1_hi, w1_lo = [sb(f"w1_{part}", [P, KT, H1], F32R) for part in ("hi", "lo")]
        w2_hi, w2_lo = [sb(f"w2_{part}", [P, O1, H2], F32R) for part in ("hi", "lo")]
        w3_sb = sb("w3_sb", [P, O2])
        b1_sb = sb("b1_sb", [P, O1])
        b2_sb = sb("b2_sb", [P, O2])
        h1 = raw[0][:, :, :].rearrange("p k d -> p (k d)").rearrange("p (o b) -> p o b", o=O1)
        h1_hi, h1_lo = [sb(f"h1_{part}", [P, O1, PB], F32R) for part in ("hi", "lo")]
        h2 = raw[1][:, 0:O2 * PB // D, :].rearrange("p k d -> p (k d)").rearrange("p (o b) -> p o b", o=O2)
        y = sb("y", [P, 1 + TILES])
        yT = e[0][0:TILES, 0, :]

        ring_ps = [psum(f"ring_ps{n}", [P, BANK // P, P]) for n in range(RB)]
        gram_ps = [psum(f"gram_ps{n}", [P, CB, BANK]) for n in range(2)]
        l2_ps = gram_ps[0][:, 0, :].rearrange("p (o b) -> p o b", o=2)
        l1_ps = [gram_ps[1][:, o % 2, (o // 2) * PB:(o // 2 + 1) * PB] for o in range(O1)]
        l3_ps = gram_ps[0][:, 1, 0:2]

        s_b = sem("biases_loaded")
        s_raw = [sem(f"raw{n}_loaded") for n in range(2)]
        s_split = sem("raw_part_split")
        s_hi = sem("raw_part_high")
        s_dense = sem("dense_loaded")
        s_ids = [sem(f"ids{h}_loaded") for h in range(2)]
        s_idx = [sem(f"ids_x{part}_loaded") for part in range(2)]
        s_gath = [[sem(f"gathered{h}_{g}") for g in range(NG)] for h in range(2)]
        s_sgo = sem("ids_load_begun")
        s_go = sem("gather_begun")
        s_pads = sem("pads_of_eT_zeroed")
        s_zero = sem("z_zeroed")
        s_id0 = sem("ident_zeroed")
        s_ident = sem("ident_ready")
        s_row = sem("row_numbers")
        s_rowf = sem("row_numbers_float")
        s_oh = sem("onehot_ready")
        s_ring = sem("ring_bank_filled")
        s_ev = sem("ring_bank_evacuated")
        s_gram = sem("gram_chunk_ready")
        s_extv = sem("gram_chunk_extracted_by_vector")
        s_exta = sem("gram_chunk_extracted_by_scalar")
        s_vgo = sem("selection_begun")
        s_mask = sem("mask_loaded")
        s_sel = sem("z_part_selected")
        s_zhi = sem("z_tile_high_part")
        s_zlo = sem("z_tile_split")
        s_l1 = sem("layer1_block_ready")
        s_h1hi = sem("h1_block_high_part")
        s_h1f = sem("h1_block_float")
        s_h1 = sem("h1_block_ready")
        s_l2 = sem("layer2_ready")
        s_h2 = sem("h2_ready")
        s_l3 = sem("layer3_ready")
        s_y = sem("y_ready")
        s_yps = sem("y_transposed")
        s_yt = sem("yT_ready")
        s_out = sem("out_stored")

        zin = z[:, 1]
        dense_rows = zin[DENSE_P:DENSE_P + DENSE, LAST_T, :]

        def rows_of(k):
            return min(P, ROWS - k * P)

        full = ROWS // P
        w1_half = KT // 2

        def raw_loads(u):
            buf = raw[u % 2]
            if u < NX:
                table = tables[ONEHOT[u]]
                return [(buf[:, 0:full, :], table[0:full * P, :].rearrange("(k p) d -> p k d", p=P)),
                        (buf[0:ROWS - full * P, full, :], table[full * P:ROWS, :])]
            flat = buf[:, :, :].rearrange("p k d -> p (k d)")
            if u < NX + 2:
                t0 = (u - NX) * w1_half
                return [(flat, w1[:, t0:t0 + w1_half, :].rearrange("p t o -> p (t o)"))]
            return [(flat.rearrange("p (k o) -> p k o", k=O1), w2.rearrange("(k p) o -> p k o", p=P))]

        def split_parts(u):
            buf = raw[u % 2]
            if u < NX:
                return [(buf[0:n, tiles, :], hi[0:n, u, tiles, :], lo[0:n, u, tiles, :])
                        for n, tiles in ((P, slice(0, full)), (ROWS - full * P, slice(full, RT)))]
            flat = buf[:, :, :].rearrange("p k d -> p (k d)")
            if u < NX + 2:
                t0 = (u - NX) * w1_half
                return [(flat, *(w[:, t0:t0 + w1_half, :].rearrange("p t o -> p (t o)") for w in (w1_hi, w1_lo)))]
            return [(flat, *(w[:, :, :].rearrange("p k o -> p (k o)") for w in (w2_hi, w2_lo)))]

        def raw_loaded(u):
            return 16 * sum(len(raw_loads(v)) for v in range(u % 2, u + 1, 2))

        def highs(u):
            return sum(len(split_parts(v)) for v in range(u + 1))

        def place(h):
            return P * (1 - h)

        def extract(copy, quads, c, h):
            n = CHUNKS * h + c
            b0 = place(h) + c * CB * GPB * Q
            samples = z[:, :, :, b0:b0 + CB * GPB * Q].rearrange("p v t (g q) -> p q g v t", q=Q)
            products = gram_ps[n % 2][:, :, :].rearrange("p a (g c) -> p (a g) c", c=P)
            for q in quads:
                own = products[SLOTS * q:SLOTS * q + NF, :, q * NF:(q + 1) * NF]
                for r in range(LAST_R + 1):
                    nt = min(KT, HALF - KT * r)
                    pairs = bass.AP(own.tensor, own.offset + KT * r,
                                    [list(own.ap[0]), list(own.ap[1]), [HALF + 1, 2], [1, nt]])
                    copy(samples[SLOTS * r:SLOTS * r + NF, q, :, :, 0:nt], pairs)
                last = copy(samples[SLOTS * LAST_R:SLOTS * LAST_R + HALF, q, :, 1, LAST_T],
                            products[SLOTS * q:SLOTS * q + HALF, :, q * NF + HALF])
            return last

        block = ctx.enter_context(nc.Block())

        @block.sync
        def _(sp):
            def load_ids(h, tile):
                sp.dma_start(idx[h][:, :], ids[bass.ds(tile * P, P), :]).then_inc(s_ids[h], 16)

            def gathers_done(h, i):
                for g in reversed(range(NG)):
                    sp.wait_ge(s_gath[h][g], 16 * len(GROUPS[g]) * (i + 1))
                    if g == NG - 1:
                        nc.sync.sem_inc(s_sgo, 1)

            def load_ids_x(i, part):
                us = (slice(0, AHEAD), slice(AHEAD, NX))[part]
                sp.dma_start(ids_x[:, us, :],
                             ids_t[us, bass.ds(i * PB, PB)].partition_broadcast(P)).then_inc(s_idx[part], 16)

            def loads(i, first=False):
                if not first:
                    sp.wait_ge(s_oh, NX * (i - 1) + AHEAD)
                    load_ids_x(i, 0)
                gathers_done(0, i - 1)
                load_ids(0, 2 * i)
                sp.wait_ge(s_oh, NX * i)
                load_ids_x(i, 1)
                gathers_done(1, i - 1)
                load_ids(1, 2 * i + 1)
                sp.wait_ge(s_zlo, 2 * i)
                sp.dma_start(dense_rows, dense_t[:, bass.ds(i * PB - P, PB)]).then_inc(s_dense, 16)

            load_ids(0, 0)
            load_ids_x(0, 0)
            for u in range(NSPLIT):
                if u >= 2:
                    sp.wait_ge(s_split, u - 1)
                for dst, src in raw_loads(u):
                    sp.dma_start(dst, src).then_inc(s_raw[u % 2], 16)
                if u == 0:
                    load_ids(1, 1)
                    load_ids_x(0, 1)
                if u == NX // 2:
                    sp.wait_ge(s_oh, AHEAD)
                    load_ids_x(1, 0)
                if u == 1:
                    sp.wait_ge(s_zero, 1)
                    sp.dma_start(dense_rows[:, P:PB], dense_t[:, 0:P]).then_inc(s_dense, 16)
                if u == 2:
                    sp.dma_start(from_low[:, :], low_half).then_inc(s_mask, 16)
            loads(1, True)
            with sp.Fori(2, PAIRS) as i:
                loads(i)
            sp.wait_ge(s_zlo, 2 * PAIRS)
            sp.dma_start(dense_rows[:, 0:P], dense_t[:, BATCH - P:BATCH]).then_inc(s_dense, 16)
            sp.wait_ge(s_yt, 1)
            sp.dma_start(out.rearrange("(t b) o -> t (b o)", b=P), yT).then_inc(s_out, 16)
            sp.wait_ge(s_out, 16)

        @block.gpsimd
        def _(pool):
            def gather_tile(h, i, first=False):
                pool.wait_ge(s_ids[h], 16 * (i + 1))
                nc.gpsimd.sem_inc(s_go, 1)
                for g, group in enumerate(GROUPS):
                    if not first:
                        pool.wait_ge(s_ring, NR * (i - 1) + RING.index(("AB"[h], g)) + 1)
                        nc.gpsimd.sem_inc(s_go, 1)
                    for s in group:
                        f = FEATURE[s]
                        pool.indirect_dma_start(
                            out=e[h][:, s, :], out_offset=None, in_=tables[f],
                            in_offset=bass.IndirectOffsetOnAxis(ap=idx[h][:, f:f + 1], axis=0),
                        ).then_inc(s_gath[h][g], 16)

            nc.gpsimd.memset(ident[:, :], 0.0).then_inc(s_id0, 1)
            nc.gpsimd.iota(row_i[:, :], pattern=[[P, RT]], base=0, channel_multiplier=1).then_inc(s_row, 1)
            pool.wait_ge(s_id0, 1)
            nc.gpsimd.affine_select(out=ident[:, :], in_=ident[:, :], compare_op=ALU.not_equal, fill=1.0,
                                    base=0, pattern=[[-1, P]], channel_multiplier=1).then_inc(s_ident, 1)
            nc.gpsimd.memset(eT[:, :, :, NF:SLOTS], 0.0).then_inc(s_pads, 1)
            gather_tile(0, 0, True)
            gather_tile(1, 0, True)
            with pool.Fori(1, PAIRS) as i:
                gather_tile(0, i)
                gather_tile(1, i)

        @block.tensor
        def _(pe):
            def split_product(out, w_hi, w_lo, x_hi, x_lo, start, stop):
                for n, (a, b) in enumerate([(w_hi, x_hi), (w_hi, x_lo), (w_lo, x_hi)]):
                    last = nc.tensor.matmul(out, a, b, start=start and n == 0, stop=stop and n == 2)
                return last

            def fill(n, i, first):
                kind, g = RING[n]
                before, steps = last_use(n, NR, RB)
                if not (first and steps):
                    pe.wait_ge(s_ev, NR * (i - steps) + before + 1)
                if kind == "X":
                    pe.wait_ge(s_oh, NX * i + g + 1)
                    if first:
                        pe.wait_ge(s_split, g + 1)
                    for k in range(RT):
                        rows = rows_of(k)
                        for part in (hi, lo):
                            last = nc.tensor.matmul(
                                ring_ps[n % RB][:, 0:2, :].rearrange("d a b -> d (a b)"),
                                part[0:rows, g, k, :], oh[g % OHB][0:rows, k, :],
                                start=(k == 0 and part is hi), stop=(k == RT - 1 and part is lo))
                else:
                    h = "AB".index(kind)
                    pe.wait_ge(s_gath[h][g], 16 * len(GROUPS[g]) * (i + 1))
                    for k, s in enumerate(GROUPS[g]):
                        last = nc.tensor.transpose(ring_ps[n % RB][:, k, :], e[h][:, s, :], ident[:, :])
                last.then_inc(s_ring, 1)

            def gram_tile(h, i, first=False):
                pe.wait_ge(s_ev, NR * i + (A_END if h == 0 else NR))
                for c in range(CHUNKS):
                    n = CHUNKS * h + c
                    if not (first and n < 2):
                        pe.wait_ge(s_extv, 2 * CHUNKS * i + n - 1)
                        pe.wait_ge(s_exta, 2 * CHUNKS * i + n - 1)
                    if n == CHUNKS + 1:
                        pe.wait_ge(s_h1f, O1 * (i + 1))
                    for k in range(CB * GPB):
                        b = (c * CB * GPB + k) * Q
                        col = (k % GPB) * P
                        slots = eT[:, h, b:b + Q, :].rearrange("d q s -> d (q s)")[:, 0:GW]
                        last = nc.tensor.matmul(gram_ps[n % 2][0:GW, k // GPB, col:col + Q * NF], slots,
                                                eT[:, h, b:b + Q, 0:NF], start=True, stop=True)
                    last.then_inc(s_gram, 1)

            def layer1(m, half, cols):
                for o in range(2 * half, 2 * half + 2):
                    if o >= 2:
                        pe.wait_ge(s_h1f, O1 * m + o - 1)
                    for t in range(KT):
                        rows, outs = slice(0, k_rows(t)), slice(o * P, (o + 1) * P)
                        last = split_product(l1_ps[o][:, cols], w1_hi[rows, t, outs], w1_lo[rows, t, outs],
                                             z_hi[rows, t, cols], z_lo[rows, t, cols], t == 0, t == KT - 1)
                    last.then_inc(s_l1, 1)

            def layer2(m, cols):
                pe.wait_ge(s_h1, O1 * (m + 1))
                for o in range(O2):
                    for k in range(O1):
                        outs = slice(o * P, (o + 1) * P)
                        last = split_product(l2_ps[:, o, cols], w2_hi[:, k, outs], w2_lo[:, k, outs],
                                             h1_hi[:, k, cols], h1_lo[:, k, cols], k == 0, k == O1 - 1)
                last.then_inc(s_l2, 1)

            def layer3(m, tiles):
                pe.wait_ge(s_h2, m + 1)
                for n in range(tiles):
                    for k in range(O2):
                        last = nc.tensor.matmul(l3_ps[:, n:n + 1], h2[:, k, n * P:(n + 1) * P],
                                                w3_sb[:, k:k + 1], start=(k == 0), stop=(k == O2 - 1))
                last.then_inc(s_l3, 1)

            def step(i, first=False):
                pair = slice(0, PB)
                for g in range(EARLY[0]):
                    fill(A_END + g, i, False)
                gram_tile(0, i, first)
                for g in range(*EARLY):
                    fill(A_END + g, i, False)
                if not first:
                    pe.wait_ge(s_extv, CHUNKS * (2 * i + 1) - 1)
                    pe.wait_ge(s_exta, CHUNKS * (2 * i + 1) - 1)
                    layer2(i - 1, pair)
                if first:
                    pe.wait_ge(s_split, NX + 2)
                    pe.wait_ge(s_b, 3 * 16)
                pe.wait_ge(s_zlo, 2 * (i + 1))
                layer1(i, 0, pair)
                if not first:
                    layer3(i - 1, 2)
                for g in range(EARLY[1], NG):
                    fill(A_END + g, i, False)
                layer1(i, 1, pair)
                if not first:
                    pe.wait_ge(s_y, i)

            pe.wait_ge(s_ident, 1)
            for n in range(A_END):
                fill(n, 0, True)
            pe.wait_ge(s_pads, 1)
            step(0, True)
            with pe.Fori(1, PAIRS) as i:
                gram_tile(1, i - 1)
                for n in range(A_END):
                    fill(n, i, False)
                step(i)
            gram_tile(1, PAIRS - 1)
            pe.wait_ge(s_extv, CHUNKS * TILES - 1)
            pe.wait_ge(s_exta, CHUNKS * TILES - 1)
            layer2(PAIRS - 1, slice(0, PB))
            pair = slice(0, PB)
            pe.wait_ge(s_zlo, 2 * PAIRS + 1)
            layer1(PAIRS, 0, pair)
            layer1(PAIRS, 1, pair)
            layer3(PAIRS - 1, 2)
            layer2(PAIRS, pair)
            pe.wait_ge(s_y, PAIRS)
            layer3(PAIRS, 1)
            pe.wait_ge(s_y, PAIRS + 1)
            nc.tensor.transpose(ring_ps[0][0:TILES, 0, :], y[:, 1:1 + TILES], ident[:, :]).then_inc(s_yps, 1)

        @block.scalar
        def _(act):
            def evacuate(n, i):
                kind, g = RING[n]
                act.wait_ge(s_ring, NR * i + n + 1)
                if kind == "X":
                    nc.scalar.copy(eT[:, :, :, NGATH + g], ring_ps[n % RB][:, 0:2, :]).then_inc(s_ev, 1)
                else:
                    h, s, ns = "AB".index(kind), GROUPS[g][0], len(GROUPS[g])
                    nc.scalar.copy(eT[:, h, :, s:s + ns].rearrange("d b s -> d s b"),
                                   ring_ps[n % RB][:, 0:ns, :]).then_inc(s_ev, 1)

            def extract_tile(h, i):
                for c in range(CHUNKS):
                    act.wait_ge(s_gram, CHUNKS * (2 * i + h) + c + 1)
                    extract(nc.scalar.copy, range(VQ, Q), c, h).then_inc(s_exta, 1)

            def round_z(h, i):
                act.wait_ge(s_sel, CHUNKS * (2 * i + h + 1))
                samples = slice(place(h), place(h) + P)
                nc.scalar.copy(z_hi[:, :, samples], zin[:, :, samples]).then_inc(s_zhi, 1)

            def relu1_hi(m, half, cols):
                for o in range(2 * half, 2 * half + 2):
                    act.wait_ge(s_l1, O1 * m + o + 1)
                    nc.scalar.activation(h1_hi[:, o, cols], l1_ps[o][:, cols], ACT.Relu,
                                         bias=b1_sb[:, o:o + 1]).then_inc(s_h1hi, 1)

            def output(m, at, tiles):
                act.wait_ge(s_l3, m + 1)
                nc.scalar.copy(y[:, at], l3_ps[:, 0:tiles]).then_inc(s_y, 1)

            def split_high(u):
                act.wait_ge(s_raw[u % 2], raw_loaded(u))
                for whole, high, low in split_parts(u):
                    nc.scalar.copy(high, whole).then_inc(s_hi, 1)

            def tile_a(i, first=False):
                for g in range(EARLY[0]):
                    evacuate(A_END + g, i)
                if first:
                    split_high(NX + 1)
                extract_tile(0, i)
                act.wait_ge(s_dense, 16 * (i + 1))
                round_z(0, i)
                if first:
                    split_high(NX + 2)
                for g in range(*EARLY):
                    evacuate(A_END + g, i)
                relu1_hi(i, 0, slice(0, PB))
                if not first:
                    output(i - 1, bass.ds(2 * i - 2, 2), 2)
                for g in range(EARLY[1], NG):
                    evacuate(A_END + g, i)
                relu1_hi(i, 1, slice(0, PB))

            act.dma_start(b1_sb[:, :], b1).then_inc(s_b, 16)
            act.dma_start(b2_sb[:, :], b2).then_inc(s_b, 16)
            act.dma_start(w3_sb[:, :], w3).then_inc(s_b, 16)
            act.wait_ge(s_zero, 1)
            nc.scalar.copy(z_hi[:, :, 0:P], zin[:, :, 0:P]).then_inc(s_zhi, 1)
            split_high(0)
            split_high(1)
            for n in range(A_END):
                if RING[n][0] == "X" and RING[n][1] < NX - 2:
                    split_high(RING[n][1] + 2)
                if RING[n] == ("X", NX - 1):
                    split_high(NX)
                evacuate(n, 0)
            act.wait_ge(s_b, 3 * 16)
            tile_a(0, True)
            with act.Fori(1, PAIRS) as i:
                extract_tile(1, i - 1)
                act.wait_ge(s_dense, 16 * (i + 1))
                round_z(1, i - 1)
                for n in range(A_END):
                    evacuate(n, i)
                tile_a(i)
            tail = slice(0, P)
            extract_tile(1, PAIRS - 1)
            act.wait_ge(s_dense, 16 * (PAIRS + 1))
            round_z(1, PAIRS - 1)
            relu1_hi(PAIRS, 0, tail)
            relu1_hi(PAIRS, 1, tail)
            output(PAIRS - 1, slice(2 * PAIRS - 2, 2 * PAIRS), 2)
            output(PAIRS, slice(2 * PAIRS, 2 * PAIRS + 1), 1)
            act.wait_ge(s_yps, 1)
            nc.scalar.copy(yT, ring_ps[0][0:TILES, 0, :]).then_inc(s_yt, 1)

        @block.vector
        def _(dve):
            def onehot(u, i):
                for k in range(RT):
                    last = nc.vector.tensor_scalar(oh[u % OHB][0:rows_of(k), k, :], ids_x[0:rows_of(k), u, :],
                                                   row_f[0:rows_of(k), k:k + 1], None, ALU.is_equal)
                last.then_inc(s_oh, 1)

            def onehots(us, i, first=False):
                for u in us:
                    before, steps = last_use(u, NX, OHB)
                    if not (first and steps):
                        dve.wait_ge(s_ring, NR * (i - steps) + RING.index(("X", before)) + 1)
                    onehot(u, i)

            def relu(out, ps, bias):
                return nc.vector.tensor_scalar(out, ps, bias, 0.0, ALU.add, ALU.max)

            def relu1(m, cols, blocks=range(O1)):
                for o in blocks:
                    dve.wait_ge(s_h1hi, O1 * m + o + 1)
                    relu(h1[:, o, cols], l1_ps[o][:, cols], b1_sb[:, o:o + 1]).then_inc(s_h1f, 1)
                    dve.wait_ge(s_h1f, O1 * m + o + 1)
                    nc.vector.tensor_tensor(h1_lo[:, o, cols], h1[:, o, cols],
                                            h1_hi[:, o, cols].bitcast(F32), ALU.subtract).then_inc(s_h1, 1)

            def relu2(m, cols):
                dve.wait_ge(s_l2, m + 1)
                for o in range(O2):
                    last = relu(h2[:, o, cols], l2_ps[:, o, cols], b2_sb[:, o:o + 1])
                last.then_inc(s_h2, 1)

            def extract_tile(h, i):
                for c in range(CHUNKS):
                    dve.wait_ge(s_gram, CHUNKS * (2 * i + h) + c + 1)
                    extract(nc.vector.tensor_copy, range(VQ), c, h).then_inc(s_extv, 1)
                    if c:
                        select(h, i, c - 1)

            def select(h, i, c):
                dve.wait_ge(s_extv, CHUNKS * (2 * i + h) + c + 1)
                dve.wait_ge(s_exta, CHUNKS * (2 * i + h) + c + 1)
                nc.vector.sem_inc(s_vgo, 1)
                nb = P // CHUNKS
                b0 = place(h) + c * nb
                for rows, nt in ((slice(0, SLOTS * LAST_R), KT), (slice(SLOTS * LAST_R, P), LAST_T)):
                    last = nc.vector.copy_predicated(
                        z[rows, 1, 0:nt, b0:b0 + nb],
                        from_low[rows, 0:nt].rearrange("p (t b) -> p t b", b=1).to_broadcast(
                            [rows.stop - rows.start, nt, nb]),
                        z[rows, 0, 0:nt, b0:b0 + nb])
                last.then_inc(s_sel, 1)

            dve.wait_ge(s_row, 1)
            nc.vector.tensor_copy(row_f[:, :], row_i[:, :]).then_inc(s_rowf, 1)
            nc.vector.memset(z[:, :, :, :], 0.0).then_inc(s_zero, 1)

            def low_z(samples, count):
                dve.wait_ge(s_zhi, count)
                nc.vector.tensor_tensor(z_lo[:, :, samples], zin[:, :, samples],
                                        z_hi[:, :, samples].bitcast(F32), ALU.subtract).then_inc(s_zlo, 1)

            def split_low(u):
                for n, (whole, high, low) in enumerate(split_parts(u)):
                    dve.wait_ge(s_hi, highs(u - 1) + n + 1)
                    last = nc.vector.tensor_tensor(low, whole, high.bitcast(F32), ALU.subtract)
                last.then_inc(s_split, 1)

            def tile_a(i, first=False):
                extract_tile(0, i)
                select(0, i, CHUNKS - 1)
                low_z(slice(P, PB), 2 * (i + 1))
                if first:
                    split_low(NX + 2)
                    dve.wait_ge(s_split, NSPLIT)
                if not first:
                    relu2(i - 1, pair)

            def ids_loaded(i, part):
                dve.wait_ge(s_idx[part], 16 * (i + 1))

            pair, tail = slice(0, PB), slice(0, P)
            dve.wait_ge(s_rowf, 1)
            for u in range(NX):
                if u in (0, AHEAD):
                    ids_loaded(0, u // AHEAD)
                onehots([u], 0, True)
                split_low(u)
            low_z(slice(0, P), 1)
            split_low(NX)
            ids_loaded(1, 0)
            onehots([0], 1)
            split_low(NX + 1)
            dve.wait_ge(s_mask, 16)
            dve.wait_ge(s_b, 3 * 16)
            tile_a(0, True)
            relu1(0, pair, range(0, 2))
            onehots(range(1, AHEAD), 1)
            relu1(0, pair, range(2, O1))
            extract_tile(1, 0)
            ids_loaded(1, 1)
            onehots([AHEAD], 1)
            select(1, 0, CHUNKS - 1)
            onehots(range(AHEAD + 1, NX), 1)
            low_z(slice(0, P), 3)
            with dve.Fori(2, PAIRS) as i:
                ids_loaded(i, 0)
                onehots(range(AHEAD), i)
                tile_a(i - 1)
                relu1(i - 1, pair)
                extract_tile(1, i - 1)
                ids_loaded(i, 1)
                onehots([AHEAD], i)
                select(1, i - 1, CHUNKS - 1)
                onehots(range(AHEAD + 1, NX), i)
                low_z(slice(0, P), 2 * i + 1)
            tile_a(PAIRS - 1)
            relu1(PAIRS - 1, pair)
            extract_tile(1, PAIRS - 1)
            select(1, PAIRS - 1, CHUNKS - 1)
            low_z(tail, 2 * PAIRS + 1)
            relu2(PAIRS - 1, pair)
            relu1(PAIRS, tail)
            relu2(PAIRS, tail)


def kernel(**inputs):
    import numpy as np
    import concourse.bacc as bacc
    from concourse.bass_utils import run_bass_kernel_spmd

    nc = bacc.Bacc("TRN2", target_bir_lowering=False, num_devices=1)
    arrays = {}

    def dram(name, a):
        a = np.ascontiguousarray(a)
        arrays[name] = a
        return nc.dram_tensor(name, a.shape, mybir.dt.from_np(a.dtype), kind="ExternalInput").ap()

    w = np.asarray(inputs["W_top1"])
    def pair(a, b):
        fi, fj = sorted((FEATURE[a], FEATURE[b]))
        return w[fj * (fj - 1) // 2 + fi]

    w1 = np.zeros((P, KT, H1), w.dtype)
    low_half = np.zeros((P, KT), np.int32)
    for n in range(HALF):
        for i in range(NF):
            p, t = SLOTS * (n // KT) + i, n % KT
            low_half[p, t] = not n <= i <= n + HALF
            if i != n:
                w1[p, t] = pair(i, n if low_half[p, t] else n + HALF + 1)
    for i in range(HALF):
        w1[SLOTS * LAST_R + i, LAST_T] = pair(i, HALF)
    w1[DENSE_P:DENSE_P + DENSE, LAST_T] = w[NF * (NF - 1) // 2:]

    args = [
        dram("dense_t", np.asarray(inputs["dense_ctx"]).T),
        dram("ids", inputs["ids"]),
        dram("ids_t", np.asarray(inputs["ids"])[:, ONEHOT].T),
        dram("low_half", low_half),
        [dram(f"tbl_{f}", inputs[f"tbl_{f}"]) for f in range(NF)],
        dram("w1", w1),
        dram("b1", np.asarray(inputs["b_top1"]).reshape(O1, P).T),
        dram("w2", inputs["W_top2"]),
        dram("b2", np.asarray(inputs["b_top2"]).reshape(O2, P).T),
        dram("w3", np.asarray(inputs["W_top3"]).reshape(O2, P).T),
    ]
    out = nc.dram_tensor("out", (BATCH, 1), F32, kind="ExternalOutput").ap()
    build(nc, *args, out)
    r = run_bass_kernel_spmd(nc, [arrays], core_ids=[0])
    return r.results[0]["out"]
```
